# Optimizing a Trainium2 kernel written in Bass

```python
import numpy as np
import jax
import jax.numpy as jnp

def _softmax(x, axis=-1):
    return jax.nn.softmax(x, axis=axis)

def _gelu(x):
    return jax.nn.gelu(x, approximate=True)

def _silu(x):
    return jax.nn.silu(x)

def _sigmoid(x):
    return jax.nn.sigmoid(x)

def _layernorm(x, axis=-1, eps=1e-05):
    m = jnp.mean(x, axis=axis, keepdims=True)
    v = jnp.var(x, axis=axis, keepdims=True)
    return (x - m) / jnp.sqrt(v + eps)

def _scatter_add(tgt, idx, src, axis=0):
    return tgt.at[idx].add(src)

def _segment_sum(src, seg, n):
    return jax.ops.segment_sum(src, seg, n)
kernel_name = 'mk_cond_seq_d2_seqx_r2_3e1bd3'

def setup_inputs(seed: int=0):
    np.random.seed(seed)
    _w = jnp.asarray

    def _rec_inputs():
        import jax
        import jax.numpy as jnp
        _rk = jax.random.key(seed)
        x = -0.0005207 + 1.001 * jax.random.normal(jax.random.fold_in(_rk, 1), (16, 512, 512), jnp.float32)
        _lenS = 512 - jax.random.randint(jax.random.fold_in(_rk, 7), (16,), 0, max(1, 512 // 4) + 1, jnp.int32)
        _lenS2 = 512 - jax.random.randint(jax.random.fold_in(_rk, 8), (16,), 0, max(1, 512 // 4) + 1, jnp.int32)
        itok_B_34_63 = jax.random.randint(jax.random.fold_in(_rk, 12), (16,), 34, 64, jnp.int32)
        fside_Bx16xSxS_0 = -1.47943e-05 + 1.00017 * jax.random.normal(jax.random.fold_in(_rk, 13), (16, 16, 512, 512), jnp.float32)
        condB_theta = jax.random.uniform(jax.random.fold_in(_rk, 14), (16,), jnp.float32, 0.0, 0.983423)
        condB_phi = jax.random.uniform(jax.random.fold_in(_rk, 15), (16,), jnp.float32, 0.0, 0.961312)
        _validS = jnp.arange(512)[None, :] < _lenS[:, None]
        _validS2 = jnp.arange(512)[None, :] < _lenS2[:, None]
        _causal = jnp.tril(jnp.ones((512, 512), dtype=bool))
        mask_Bx1xSxS_bk0 = jnp.logical_not(jnp.broadcast_to(_validS[:, None, None, :], (16, 1, 512, 512)))
        return (x, itok_B_34_63, fside_Bx16xSxS_0, condB_theta, condB_phi, mask_Bx1xSxS_bk0)
    x, itok_B_34_63, fside_Bx16xSxS_0, condB_theta, condB_phi, mask_Bx1xSxS_bk0 = _rec_inputs()

    def _L0_cond_setup():
        import jax, jax.numpy as jnp
        import numpy as np
        import math
        D_MODEL = 512
        N_HEAD = 16
        HEAD_DIM = D_MODEL // N_HEAD
        D_FF = 2048
        NUM_STEPS = 100.0
        RESCALE = 4000.0
        EPS = 1e-05

        def _sin_emb(t):
            half = D_MODEL // 2
            x = t.astype(jnp.float32) / NUM_STEPS * RESCALE
            freqs = jnp.exp(jnp.arange(half, dtype=jnp.float32) * (-math.log(10000.0) / (half - 1)))
            e = x[:, None] * freqs[None, :]
            return jnp.concatenate([jnp.sin(e), jnp.cos(e)], axis=-1)

        def _ln(x):
            m = jnp.mean(x, axis=-1, keepdims=True)
            v = jnp.var(x, axis=-1, keepdims=True)
            return (x - m) / jnp.sqrt(v + EPS)

        def _gelu2(x):
            return x * jax.nn.sigmoid(1.702 * x)
        key = jax.random.key(seed)
        ks = jax.random.split(key, 24)
        B, S, D, F = (4, 256, D_MODEL, D_FF)
        std = 0.02
        inp = {'src': jax.random.normal(ks[0], (B, S, D), dtype=jnp.float32), 'src_mask': jax.random.randint(ks[1], (B, 1, S, S), 0, 2).astype(bool), 'timestep': jax.random.randint(ks[2], (B,), 0, 100, dtype=jnp.int32), 'attention_bias': jax.random.normal(ks[3], (B, N_HEAD, S, S), dtype=jnp.float32), 'W_ada': jax.random.normal(ks[4], (D, 2 * D), dtype=jnp.float32) * std, 'b_ada': jnp.zeros((2 * D,), dtype=jnp.float32), 'Wq': jax.random.normal(ks[5], (D, D), dtype=jnp.float32) * std, 'bq': jnp.zeros((D,), dtype=jnp.float32), 'Wk': jax.random.normal(ks[6], (D, D), dtype=jnp.float32) * std, 'bk': jnp.zeros((D,), dtype=jnp.float32), 'Wv': jax.random.normal(ks[7], (D, D), dtype=jnp.float32) * std, 'bv': jnp.zeros((D,), dtype=jnp.float32), 'Wo': jax.random.normal(ks[8], (D, D), dtype=jnp.float32) * std, 'bo': jnp.zeros((D,), dtype=jnp.float32), 'W1': jax.random.normal(ks[9], (D, F), dtype=jnp.float32) * std, 'b1': jnp.zeros((F,), dtype=jnp.float32), 'W2': jax.random.normal(ks[10], (F, D), dtype=jnp.float32) * std, 'b2': jnp.zeros((D,), dtype=jnp.float32), 'g2': jnp.ones((D,), dtype=jnp.float32), 'beta2': jnp.zeros((D,), dtype=jnp.float32)}
        return inp
    _L0_cond_all = _L0_cond_setup()
    _L0_cond_in = {k: v for k, v in _L0_cond_all.items() if k in ('W_ada', 'b_ada', 'Wq', 'bq', 'Wk', 'bk', 'Wv', 'bv', 'Wo', 'bo', 'W1', 'b1', 'W2', 'b2', 'g2', 'beta2')}
    del _L0_cond_all

    def _L1_cond_setup():
        import jax, jax.numpy as jnp
        import numpy as np
        key = jax.random.key(seed)
        k1, k2, k3 = jax.random.split(key, 3)
        B, N, D = (16, 2048, 512)
        embeddings = jax.random.normal(k1, (B, N, D), dtype=jnp.float32)
        theta = jax.random.uniform(k2, (B,), dtype=jnp.float32)
        phi = jax.random.uniform(k3, (B,), dtype=jnp.float32)
        return {'embeddings': embeddings, 'theta': theta, 'phi': phi}
    _L1_cond_all = _L1_cond_setup()
    _L1_cond_in = {k: v for k, v in _L1_cond_all.items() if k in ()}
    del _L1_cond_all
    return {'x': x, 'itok_B_34_63': itok_B_34_63, 'fside_Bx16xSxS_0': fside_Bx16xSxS_0, 'condB_theta': condB_theta, 'condB_phi': condB_phi, 'mask_Bx1xSxS_bk0': mask_Bx1xSxS_bk0, 'L0_cond_W_ada': _L0_cond_in['W_ada'], 'L0_cond_b_ada': _L0_cond_in['b_ada'], 'L0_cond_Wq': _L0_cond_in['Wq'], 'L0_cond_bq': _L0_cond_in['bq'], 'L0_cond_Wk': _L0_cond_in['Wk'], 'L0_cond_bk': _L0_cond_in['bk'], 'L0_cond_Wv': _L0_cond_in['Wv'], 'L0_cond_bv': _L0_cond_in['bv'], 'L0_cond_Wo': _L0_cond_in['Wo'], 'L0_cond_bo': _L0_cond_in['bo'], 'L0_cond_W1': _L0_cond_in['W1'], 'L0_cond_b1': _L0_cond_in['b1'], 'L0_cond_W2': _L0_cond_in['W2'], 'L0_cond_b2': _L0_cond_in['b2'], 'L0_cond_g2': _L0_cond_in['g2'], 'L0_cond_beta2': _L0_cond_in['beta2']}

def reference(x, itok_B_34_63, fside_Bx16xSxS_0, condB_theta, condB_phi, mask_Bx1xSxS_bk0, L0_cond_W_ada, L0_cond_b_ada, L0_cond_Wq, L0_cond_bq, L0_cond_Wk, L0_cond_bk, L0_cond_Wv, L0_cond_bv, L0_cond_Wo, L0_cond_bo, L0_cond_W1, L0_cond_b1, L0_cond_W2, L0_cond_b2, L0_cond_g2, L0_cond_beta2):
    import jax
    import jax.numpy as jnp

    def _L0_cond_ref(src, src_mask, timestep, attention_bias, W_ada, b_ada, Wq, bq, Wk, bk, Wv, bv, Wo, bo, W1, b1, W2, b2, g2, beta2):
        import jax, jax.numpy as jnp
        import numpy as np
        import math
        D_MODEL = 512
        N_HEAD = 16
        HEAD_DIM = D_MODEL // N_HEAD
        D_FF = 2048
        NUM_STEPS = 100.0
        RESCALE = 4000.0
        EPS = 1e-05

        def _sin_emb(t):
            half = D_MODEL // 2
            x = t.astype(jnp.float32) / NUM_STEPS * RESCALE
            freqs = jnp.exp(jnp.arange(half, dtype=jnp.float32) * (-math.log(10000.0) / (half - 1)))
            e = x[:, None] * freqs[None, :]
            return jnp.concatenate([jnp.sin(e), jnp.cos(e)], axis=-1)

        def _ln(x):
            m = jnp.mean(x, axis=-1, keepdims=True)
            v = jnp.var(x, axis=-1, keepdims=True)
            return (x - m) / jnp.sqrt(v + EPS)

        def _gelu2(x):
            return x * jax.nn.sigmoid(1.702 * x)
        B, S, D = src.shape
        emb = jax.nn.silu(_sin_emb(timestep)) @ W_ada + b_ada
        scale, shift = jnp.split(emb[:, None, :], 2, axis=-1)
        x = _ln(src) * (1.0 + scale) + shift
        q = (x @ Wq + bq).reshape(B, S, N_HEAD, HEAD_DIM).transpose(0, 2, 1, 3)
        k = (x @ Wk + bk).reshape(B, S, N_HEAD, HEAD_DIM).transpose(0, 2, 1, 3)
        v = (x @ Wv + bv).reshape(B, S, N_HEAD, HEAD_DIM).transpose(0, 2, 1, 3)
        scores = jnp.einsum('bhqd,bhkd->bhqk', q / math.sqrt(HEAD_DIM), k)
        scores = scores + attention_bias
        scores = jnp.where(src_mask, -jnp.inf, scores.astype(jnp.float32))
        probs = jax.nn.softmax(scores, axis=-1).astype(v.dtype)
        ctx = jnp.einsum('bhqk,bhkd->bhqd', probs, v)
        ctx = ctx.transpose(0, 2, 1, 3).reshape(B, S, D)
        x = x + (ctx @ Wo + bo)
        h = _ln(x) * g2 + beta2
        ff = _gelu2(h @ W1 + b1) @ W2 + b2
        return x + ff

    def _L1_cond_ref(embeddings, theta, phi):
        import jax, jax.numpy as jnp
        import numpy as np
        B, N, D = embeddings.shape
        e = embeddings.reshape(B, N, D // 4, 4)
        ct = jnp.cos(theta)[:, None, None]
        st = jnp.sin(theta)[:, None, None]
        cp = jnp.cos(phi)[:, None, None]
        sp = jnp.sin(phi)[:, None, None]
        x0, x1, x2, x3 = (e[..., 0], e[..., 1], e[..., 2], e[..., 3])
        out = jnp.stack([x0 * ct + x1 * st, -x0 * st + x1 * ct, x2 * cp + x3 * sp, -x2 * sp + x3 * cp], axis=-1)
        return out.reshape(B, N, D)
    x = _L0_cond_ref(x, mask_Bx1xSxS_bk0, itok_B_34_63, fside_Bx16xSxS_0, L0_cond_W_ada, L0_cond_b_ada, L0_cond_Wq, L0_cond_bq, L0_cond_Wk, L0_cond_bk, L0_cond_Wv, L0_cond_bv, L0_cond_Wo, L0_cond_bo, L0_cond_W1, L0_cond_b1, L0_cond_W2, L0_cond_b2, L0_cond_g2, L0_cond_beta2)
    x = _L1_cond_ref(x, condB_theta, condB_phi)
    return x

_drawn_inputs = setup_inputs


def setup_inputs(seed=0):
    import zlib

    import numpy as np

    out = dict(_drawn_inputs(seed))
    spreads = {'L0_cond_b_ada': (0.0, 0.1),
     'L0_cond_bq': (0.0, 0.8),
     'L0_cond_bk': (0.0, 0.8),
     'L0_cond_bv': (0.0, 0.1),
     'L0_cond_bo': (0.0, 0.1),
     'L0_cond_b1': (0.0, 0.1),
     'L0_cond_b2': (0.0, 0.1),
     'L0_cond_g2': (1.0, 0.2),
     'L0_cond_beta2': (0.0, 0.36)}
    factors = {'fside_Bx16xSxS_0': 4.512, 'L0_cond_Wq': 8.0, 'L0_cond_Wk': 8.0}
    for name, (base, spread) in spreads.items():
        noise = np.random.default_rng([zlib.crc32(name.encode()), seed]).standard_normal(out[name].shape)
        drawn = base * np.exp(spread * noise) if base else spread * noise
        out[name] = jnp.asarray(drawn.astype(out[name].dtype))
    for name, factor in factors.items():
        out[name] = (out[name] * factor).astype(out[name].dtype)
    return out
```

```python
import math
from contextlib import ExitStack

import numpy as np
import concourse.bass as bass
from concourse import mybir
from concourse.alu_op_type import AluOpType as ALU

F32 = mybir.dt.float32
F32R = mybir.dt.float32r
BF16 = mybir.dt.bfloat16
I32 = mybir.dt.int32
U8 = mybir.dt.uint8
ACT = mybir.ActivationFunctionType

P = 128
EPS = 1e-5
SIGMOID_RATE = 1.702
MASKED = -3.0e38
LOWEST = 3.0e38
ROUND = 12582912.0
TWO_PI_1 = 6.28125
TWO_PI_2 = float(np.float32(round((2 * math.pi - TWO_PI_1) * 2**20) / 2**20))
TWO_PI_3 = 2 * math.pi - TWO_PI_1 - TWO_PI_2
NUM_STEPS, RESCALE = 100.0, 4000.0


class Tally:

    def __init__(self, sem, per, unit=1):
        self.sem, self.per, self.unit = sem, per, unit

    def at(self, batch, index):
        return (batch + 1) * (self.per * self.unit) + (index + 1) * self.unit

    def wait(self, eng, batch, index):
        eng.wait_ge(self.sem, self.at(batch, index))

    def credit(self, eng, events):
        eng.sem_inc(self.sem, events * self.unit)


def layer_program(nc, x, steps, bias, theta, phi, mask, W_ada, b_ada, Wq, bq, Wk, bk, Wv, bv, Wo, bo,
                  W1, b1, W2, b2, g2, beta2, freqs, out):
    B, S, D = x.shape
    H = bias.shape[1]
    F = W1.shape[1]
    NT, NC = S // P, D // P
    assert (S, D, H, F % P) == (512, 512, 16, 0) and B > 2

    ctx_dram = nc.dram_tensor("context_t", (B, D, S), F32, kind="Internal").ap()
    xmod_dram = nc.dram_tensor("modulated_t", (B, D, S), F32, kind="Internal").ap()

    whole = ExitStack()
    with whole:
        def keep(name, shape, dt=F32):
            return whole.enter_context(nc.sbuf_tensor(name, shape, dt))

        ident = keep("ident", [P, P])
        mod = keep("mod", [P, 2, NC, B])
        rot = keep("rot", [P, 6, B])
        half_pow = keep("half_pow", [P, NT])
        with ExitStack() as stage:
            attention_stage(nc, stage, x, steps, bias, theta, phi, mask, W_ada, b_ada, (Wq, Wk, Wv), (bq, bk, bv),
                            freqs, ident, mod, rot, half_pow, ctx_dram, xmod_dram)
        with ExitStack() as stage:
            ffn_stage(nc, stage, W1, b1, W2, b2, g2, beta2, Wo, bo, ident, rot, half_pow, ctx_dram, xmod_dram, out)


def setup_block(nc, steps, theta, phi, W_ada, b_ada, W_qkv, b_qkv, freqs, ident, mod, rot, half_pow, WH, WL, bqk,
                bv_rows):
    B = steps.shape[0]
    D = W_ada.shape[0]
    NC = D // P
    NE = 2 * NC
    HALF = NC // 2
    QSCALE = 1.0 / math.sqrt(32)
    PI_BELOW = 3.1415925

    with ExitStack() as local:
        def sb(name, shape, dt=F32):
            return local.enter_context(nc.sbuf_tensor(name, shape, dt))

        def sem(name):
            return local.enter_context(nc.semaphore(name))

        wada = sb("wada", [P, NC, 2 * D])
        wst = sb("wst", [P, 3, NC, D])
        NA = HALF + 2
        ang = sb("ang", [P, 2 * NA, B])
        turns = sb("turns", [P, 2 * NA, B])
        trig = sb("trig", [P, 2 * NA, B])
        trig_tanh = sb("trig_tanh", [P, 2 * NA, B])
        silu2 = sb("silu2", [P, 2 * NA, B])
        ti = sb("ti", [P, B], I32)
        tf, tq, tr = (sb(n, [P, B]) for n in ("tf", "tq", "tr"))
        fr = sb("fr", [P, HALF])
        bada = sb("bada", [P, NE])
        bqk_in = sb("bqk_in", [P, 2, NC])
        ps = local.enter_context(nc.psum_tensor("ps_setup", [P, 512], F32))
        small_in, wada_in, late_in = sem("small_in"), sem("wada_in"), sem("late_in")
        w_in = [sem(f"w_in{i}") for i in range(3)]
        made, act_made, tab, pooled, scaled = (sem(n) for n in ("made", "act_made", "ada_done", "pooled", "scaled"))

        with nc.Block() as block:

            @block.sync
            def _(sp):
                sp.dma_start(ti[:, :], steps.unsqueeze(0).broadcast_to([P, B])).then_inc(small_in, 16)
                sp.dma_start(fr[:, :], freqs.rearrange("(c p) -> p c", p=P), allow_slow_non_contiguous=True)\
                    .then_inc(small_in, 16)
                for n, angle in enumerate((theta, phi)):
                    for half in range(2):
                        sp.dma_start(ang[:, half * NA + HALF + n, :], angle.unsqueeze(0).broadcast_to([P, B]))\
                            .then_inc(small_in, 16)
                sp.dma_start(wada[:, :, :], W_ada.rearrange("(c p) d -> p c d", p=P)).then_inc(wada_in, 16)
                sp.dma_start(bada[:, :], b_ada.rearrange("(c p) -> p c", p=P), allow_slow_non_contiguous=True)\
                    .then_inc(late_in, 16)
                for n in range(2):
                    sp.dma_start(bqk_in[:, n, :], b_qkv[n].rearrange("(c p) -> p c", p=P),
                                 allow_slow_non_contiguous=True).then_inc(late_in, 16)
                sp.dma_start(bv_rows[:, :], b_qkv[2].unsqueeze(0).broadcast_to([P, D])).then_inc(late_in, 16)
                for n in range(3):
                    sp.dma_start(wst[:, n, :, :], W_qkv[n].rearrange("(c p) d -> p c d", p=P)).then_inc(w_in[n], 16)

            @block.gpsimd
            def _(pool):
                pool.memset(ident[:, :], 0.0).then_inc(pooled, 1)
                pool.memset(half_pow[:, :], -0.5).then_inc(pooled, 1)
                pool.wait_ge(pooled, 2)
                pool.affine_select(out=ident[:, :], in_=ident[:, :], compare_op=ALU.not_equal, fill=1.0, base=0,
                                   pattern=[[-1, P]], channel_multiplier=1).then_inc(pooled, 1)

            @block.vector
            def _(dve):
                dve.wait_ge(small_in, 16 * 6)
                dve.tensor_copy(tf[:, :], ti[:, :]).then_inc(made, 1)
                dve.wait_ge(made, 1)
                dve.tensor_scalar(tq[:, :], tf[:, :], 1.0 / NUM_STEPS, None, ALU.mult).then_inc(made, 1)
                dve.wait_ge(made, 2)
                dve.scalar_tensor_tensor(tr[:, :], tq[:, :], -64.0, tf[:, :], ALU.mult, ALU.add).then_inc(made, 1)
                dve.wait_ge(made, 3)
                dve.scalar_tensor_tensor(tr[:, :], tq[:, :], -32.0, tr[:, :], ALU.mult, ALU.add).then_inc(made, 1)
                dve.wait_ge(made, 4)
                dve.scalar_tensor_tensor(tr[:, :], tq[:, :], -4.0, tr[:, :], ALU.mult, ALU.add).then_inc(made, 1)
                dve.wait_ge(made, 5)
                dve.scalar_tensor_tensor(tq[:, :], tr[:, :], 1.0 / NUM_STEPS, tq[:, :], ALU.mult, ALU.add)\
                    .then_inc(made, 1)
                dve.wait_ge(made, 6)
                dve.tensor_scalar(tq[:, :], tq[:, :], RESCALE, None, ALU.mult).then_inc(made, 1)
                dve.wait_ge(made, 7)
                for half in range(2):
                    for c in range(HALF):
                        dve.tensor_scalar(ang[:, half * NA + c, :], tq[:, :], fr[:, c:c + 1], None, ALU.mult)\
                            .then_inc(made, 1)
                dve.wait_ge(made, 11)
                dve.tensor_scalar(turns[:, :NA, :], ang[:, :NA, :], 1.0 / (2 * math.pi), None, ALU.mult)\
                    .then_inc(made, 1)
                dve.tensor_scalar(turns[:, NA:, :], ang[:, NA:, :], 1.0 / (2 * math.pi), 0.25, ALU.mult, ALU.add)\
                    .then_inc(made, 1)
                dve.wait_ge(made, 13)
                dve.tensor_scalar(turns[:, :, :], turns[:, :, :], ROUND, None, ALU.add).then_inc(made, 1)
                dve.wait_ge(made, 14)
                dve.tensor_scalar(turns[:, :, :], turns[:, :, :], -ROUND, None, ALU.add).then_inc(made, 1)
                for n, part in enumerate((TWO_PI_1, TWO_PI_2, TWO_PI_3)):
                    dve.wait_ge(made, 15 + n)
                    dve.scalar_tensor_tensor(ang[:, :, :], turns[:, :, :], -part, ang[:, :, :], ALU.mult, ALU.add)\
                        .then_inc(made, 1)
                dve.wait_ge(made, 18)
                dve.tensor_scalar(ang[:, NA:, :], ang[:, NA:, :], math.pi / 2, None, ALU.add).then_inc(made, 1)
                dve.wait_ge(made, 19)
                dve.tensor_scalar(ang[:, :, :], ang[:, :, :], PI_BELOW, -PI_BELOW, ALU.min, ALU.max)\
                    .then_inc(made, 1)
                dve.wait_ge(act_made, 2)
                dve.tensor_copy(rot[:, 0:2, :], trig[:, HALF:NA, :]).then_inc(made, 1)
                dve.tensor_copy(rot[:, 2:4, :], trig[:, NA + HALF:, :]).then_inc(made, 1)
                dve.scalar_tensor_tensor(silu2[:, :, :], trig_tanh[:, :, :], 1.0, trig[:, :, :], ALU.add, ALU.mult)\
                    .then_inc(made, 1)
                dve.wait_ge(made, 23)
                dve.tensor_scalar(silu2[:, :, :], silu2[:, :, :], 0.5, None, ALU.mult).then_inc(made, 1)
                dve.wait_ge(tab, 1)
                dve.wait_ge(late_in, 16 * 4)
                dve.tensor_tensor(mod[:, :, :, :].rearrange("p a c b -> p (a c) b"),
                                  ps[:, 0:NE * B].rearrange("p (c b) -> p c b", b=B),
                                  bada[:, :].unsqueeze(2).broadcast_to([P, NE, B]), ALU.add).then_inc(made, 1)
                dve.tensor_scalar(rot[:, 4:6, :], rot[:, 0:2, :], -1.0, None, ALU.mult)
                dve.wait_ge(made, 25)
                dve.tensor_scalar(mod[:, 0, :, :], mod[:, 0, :, :], 1.0, None, ALU.add).then_inc(made, 1)
                dve.tensor_scalar(bqk[:, 0, :], bqk_in[:, 0, :], QSCALE, None, ALU.mult).then_inc(made, 1)
                dve.tensor_copy(bqk[:, 1, :], bqk_in[:, 1, :]).then_inc(made, 1)
                for n in range(3):
                    dve.wait_ge(scaled, 1 + NC * (n + 1))
                    for c in range(NC):
                        dve.tensor_tensor(WL[n][:, c, :], wst[:, n, c, :], WH[n][:, c, :].bitcast(F32), ALU.subtract)

            @block.scalar
            def _(act):
                act.wait_ge(made, 20)
                act.activation(trig[:, :, :], ang[:, :, :], ACT.Sin).then_inc(act_made, 1)
                act.wait_ge(act_made, 1)
                act.activation(trig_tanh[:, :, :], trig[:, :, :], ACT.Tanh, scale=0.5).then_inc(act_made, 1)
                act.wait_ge(w_in[0], 16)
                act.mul(wst[:, 0, :, :], wst[:, 0, :, :], QSCALE).then_inc(scaled, 1)
                act.wait_ge(scaled, 1)
                for n in range(3):
                    act.wait_ge(w_in[n], 16)
                    for c in range(NC):
                        act.activation(WH[n][:, c, :], wst[:, n, c, :], ACT.Copy).then_inc(scaled, 1)

            @block.tensor
            def _(pe):
                pe.wait_ge(wada_in, 16)
                pe.wait_ge(made, 24)
                for o in range(NE):
                    for c in range(NC):
                        e = c if c < HALF else NA + c - HALF
                        mm = pe.matmul(ps[:, o * B:(o + 1) * B], wada[:, c, o * P:(o + 1) * P], silu2[:, e, :],
                                       start=(c == 0), stop=(c == NC - 1))
                mm.then_inc(tab, 1)


def attention_stage(nc, stage, x, steps, bias, theta, phi, mask, W_ada, b_ada, W_qkv, b_qkv, freqs, ident, mod, rot,
                    half_pow, ctx_dram, xmod_dram):
    B, S, D = x.shape
    H = bias.shape[1]
    HD = D // H
    NT = S // P
    NC = D // P
    GH = P // HD
    NG = H // GH

    def sb(name, shape, dt=F32):
        return stage.enter_context(nc.sbuf_tensor(name, shape, dt))

    def sem(name):
        return stage.enter_context(nc.semaphore(name))

    WH = [sb(f"w{n}_hi", [P, NC, D], F32R) for n in "qkv"]
    WL = [sb(f"w{n}_lo", [P, NC, D], F32R) for n in "qkv"]
    bqk = sb("bqk", [P, 2, NG])
    bv_rows = sb("bv_rows", [P, D])

    setup_block(nc, steps, theta, phi, W_ada, b_ada, W_qkv, b_qkv, freqs, ident, mod, rot, half_pow, WH, WL, bqk, bv_rows)

    xn = sb("xn", [P, NT, D])
    xf = sb("xf", [P, 2, S])
    XH = sb("x_hi", [P, NC, S], F32R)
    XL = sb("x_lo", [P, NC, S], F32R)
    hi = [sb(f"{n}_hi", [P, S], F32R) for n in "qk"]
    lo = [sb(f"{n}_lo", [P, S], F32R) for n in "qk"]
    stacked = [[sb(f"{n}_rows{i}", [3 * HD, GH, S], F32R) for i in range(2)] for n in "qk"]
    V = sb("v", [P, NT, D])
    prob = sb("prob", [P, 2, NT, S])
    probT = sb("probT", [P, GH, NT, S])
    biasm = sb("biasm", [P, 2, NT, S])
    mask_raw = sb("mask_raw", [P, NT, S // 4], I32)
    maskb = sb("maskb", [P, NT, S], BF16)
    negmax = sb("negmax", [P, 2, NT])
    sums = sb("sums", [P, 2, NT, GH])
    rsum = sb("rsum", [P, NT, GH])
    rsum_wide = sb("rsum_wide", [P, NT, GH, HD])
    rsumT = sb("rsumT", [P, 2, S])
    stats = sb("stats", [P, NT, 6])
    mean_var = sb("mean_var", [P, NT, 2])
    var_eps = sb("var_eps", [P, NT])
    rstd = sb("rstd", [P, NT])
    mod_now = sb("mod_now", [P, 2, NC])

    def bank(name, n=1):
        t = stage.enter_context(nc.psum_tensor(name, [P, n, 512], F32))
        return t

    ps_score = bank("ps_score", 2)
    ps_probT = bank("ps_probT", 2)
    ps_ctx = bank("ps_ctx")
    ps_fill = bank("ps_fill", 2)
    ps_rsum = bank("ps_rsum")

    dve_waited, pool_waited = sem("dve_waited"), sem("pool_waited")
    TL = H * NT
    scored = Tally(sem("scored"), TL)
    maxed = Tally(sem("maxed"), TL)
    exped = Tally(sem("exped"), TL)
    turned = Tally(sem("turned"), TL)
    outT_act = Tally(sem("outT_act"), TL // 2)
    outT_dve = Tally(sem("outT_dve"), TL // 2)
    pv_done = Tally(sem("pv_done"), NG * NT)
    masked = Tally(sem("masked"), TL // 2)
    mask_ready = Tally(sem("mask_ready"), 1)
    pow_done = Tally(sem("pow_done"), 1)
    stats_done = Tally(sem("stats_done"), 1)
    dve_step = sem("dve_step")
    normed = Tally(sem("normed"), NT)
    xt_done = Tally(sem("xt_done"), NC)
    xf_done = Tally(sem("xf_done"), NC)
    xh_done = Tally(sem("xh_done"), NC)
    xl_done = Tally(sem("xl_done"), NC)
    mod_done = Tally(sem("mod_done"), 1)
    proj_done = Tally(sem("proj_done"), 2 * NG)
    hi_done = Tally(sem("hi_done"), 2 * NG)
    lo_done = Tally(sem("lo_done"), 2 * NG)
    vproj_done = Tally(sem("vproj_done"), NT)
    v_done = Tally(sem("v_done"), NT)
    rsum_done = Tally(sem("rsum_done"), NG)
    wide_done = Tally(sem("wide_done"), NG)
    rt_done = Tally(sem("rt_done"), NG)
    rt_out = Tally(sem("rt_out"), NG)
    ctx_done = Tally(sem("ctx_done"), NG)
    x_in = Tally(sem("x_in"), 1, 16)
    mask_in = Tally(sem("mask_in"), 1, 16)
    bias_in = [Tally(sem(f"bias_in{s}"), TL // 8, 16) for s in range(4)]
    rows_in = [[Tally(sem(f"{n}_rows_in{i}"), NG // 2, 16 * 3 * GH) for i in range(2)] for n in "qk"]
    ctx_out = [Tally(sem(f"ctx_out{i}"), NG // 2, 16) for i in range(2)]
    xmod_out = [Tally(sem(f"xmod_out{i}"), NC // 2, 16) for i in range(2)]

    fillers = {1: [("v", 0), ("v", 1)], 2: [("v", 2)], 3: [("v", 3), ("q", 2)],
               7: [("q", 3)], 9: [("x", 0), ("x", 1)], 10: [("x", 2), ("x", 3)],
               11: [("q", 4)], 15: [("q", 5)]}
    for g in range(NG):
        fillers[4 * g] = [("k", g + 1)]
    order = [(j, f) for j in sorted(fillers) for f in fillers[j]]
    qk_order = [f for _, f in order if f[0] in "qk"]
    assert len(order) % 2 == 0 and len(qk_order) == 2 * NG

    START, FIRST, MIDDLE, LAST, END = "start", "first", "middle", "last", "end"
    WHOLE = (FIRST, MIDDLE, LAST)
    AHEAD = (START, FIRST, MIDDLE)

    def runs(mode, j, f):
        if mode in (FIRST, MIDDLE):
            return True
        ahead = f[0] == "x" or (f[0] in "qk" and f[1] >= NG)
        return ahead if mode == START else (not ahead if mode == LAST else False)

    def slots(mode):
        heads = range(2) if mode == END else range(H)
        return [(j, i) for j in heads for i in range(NT)]

    def fills_at(mode, j, i):
        fs = fillers.get(j, [])
        at = {1: [1], 2: [0, 2]}.get(len(fs), [])
        return [f for f, a in zip(fs, at) if a == i and runs(mode, j, f)]

    def score_tile(mode, b, j, i):
        if j + 1 < H:
            return (b, j + 1, i) if mode in WHOLE else None
        return (b + 1, 0, i) if mode in AHEAD else None

    def group_before(mode, b, g):
        if mode == START or (mode, g) == (FIRST, 0) or (mode == END and g > 0):
            return None
        return (b - 1, NG - 1) if g == 0 else (b, g - 1)

    def group_of(f):
        n = f[1]
        return n // NG, n % NG, n % 2

    def batches(eng, body):
        body(START, -1)
        body(FIRST, 0)
        with eng.Fori(1, B - 1) as b:
            body(MIDDLE, b)
        body(LAST, B - 1)
        body(END, B)

    def rows_event(q, b, g):
        if q == 1 and g % 2 == 1:
            return (b, g // 2)
        return (b - 1, 1) if g < 2 else (b, 0)

    def previous_rows(mode, b, f):
        same = [x for x in qk_order if x[0] == f[0]]
        k = same.index(f)
        if k > 0:
            if not (mode == START and same[k - 1][1] < NG):
                prev, pb = same[k - 1], b
            else:
                return None
        else:
            if mode == START:
                return None
            prev, pb = same[-1], b - 1
        q = "qk".index(f[0])
        ahead, g, buf = group_of(prev)
        rb, ri = rows_event(q, pb + ahead, g)
        return rows_in[q][buf], rb, ri

    with nc.Block() as block:

        @block.sync
        def _(sp):
            def load_bias(b, u):
                h, half = u // 2, u % 2
                src = bias[bass.ds(b, 1), h, 2 * half * P:2 * (half + 1) * P, :].rearrange("o (t p) k -> p (o t) k", p=P)
                sp.dma_start(biasm[:, h % 2, 2 * half:2 * half + 2, :], src).then_inc(bias_in[u % 4].sem, 16)

            def load_x(b):
                sp.dma_start(xn[:, :, :], x[bass.ds(b, 1), :, :].rearrange("o (t p) d -> p (o t) d", p=P)).then_inc(x_in.sem, 16)

            def load_mask(b):
                sp.dma_start(mask_raw[:, :, :], mask[bass.ds(b, 1), 0, :, :].rearrange("o (t p) k -> p (o t) k", p=P)).then_inc(mask_in.sem, 16)

            def body(mode, b):
                if mode == START:
                    for q, buf in ((0, 0), (0, 1), (1, 0), (1, 1), (1, 1)):
                        rows_in[q][buf].credit(sp, 1)
                    for s in range(4):
                        bias_in[s].credit(sp, TL // 8)
                    for s in range(2):
                        ctx_out[s].credit(sp, NG // 2)
                    ctx_out[0].credit(sp, 1)
                    load_x(0)
                    load_mask(0)
                    for u in range(4):
                        load_bias(0, u)
                for j, i in slots(mode):
                    t = score_tile(mode, b, j, i)
                    if t is not None and i % 2 == 1:
                        u = 2 * t[1] + i // 2 + 4
                        nb, nu = (t[0], u) if u < 2 * H else (t[0] + 1, u - 2 * H)
                        if not (mode == LAST and u >= 2 * H):
                            maxed.wait(sp, t[0], NT * t[1] + i)
                            load_bias(nb, nu)
                    for f in fills_at(mode, j, i):
                        if f[0] in "qk":
                            q = "qk".index(f[0])
                            ahead, g, buf = group_of(f)
                            n = qk_order.index(f)
                            lo_done.wait(sp, b, n)
                            if mode != START:
                                if g >= 2:
                                    scored.wait(sp, b + ahead, GH * (g - 2) * NT + GH * NT - 1)
                                else:
                                    scored.wait(sp, b + ahead - 1, GH * (g + 2) * NT + GH * NT - 1)
                            parts = [hi[q], hi[q], lo[q]] if q == 0 else [hi[q], lo[q], hi[q]]
                            for r, part in enumerate(parts):
                                for h in range(GH):
                                    sp.dma_start(stacked[q][buf][HD * r:HD * (r + 1), h, :].bitcast(F32),
                                                 part[HD * h:HD * (h + 1), :].bitcast(F32)).then_inc(rows_in[q][buf].sem, 16)
                        if f[0] == "x":
                            c = f[1]
                            xf_done.wait(sp, b, c)
                            sp.dma_start(xmod_dram[bass.ds(b + 1, 1), c * P:(c + 1) * P, :].rearrange("o p s -> p (o s)"),
                                         xf[:, c % 2, :]).then_inc(xmod_out[c % 2].sem, 16)
                    if (j, i) == (1, 0) and mode in (FIRST, MIDDLE):
                        xt_done.wait(sp, b - 1, NC - 1)
                        load_x(b + 1)
                        mask_ready.wait(sp, b, 0)
                        load_mask(b + 1)
                    g = j // GH
                    before = group_before(mode, b, g)
                    if (j % GH, i) == (1, 2) and before is not None:
                        ctx_done.wait(sp, b, g)
                        cb, cg = before
                        sp.dma_start(ctx_dram[bass.ds(cb, 1), cg * P:(cg + 1) * P, :].rearrange("o p s -> p (o s)"),
                                     rsumT[:, g % 2, :]).then_inc(ctx_out[g % 2].sem, 16)
                if mode == END:
                    ctx_out[0].wait(sp, B, 0)
                    ctx_out[1].wait(sp, B - 1, NG // 2 - 1)
                    for s in range(2):
                        xmod_out[s].wait(sp, B - 2, NC // 2 - 1)

            batches(sp, body)

        @block.gpsimd
        def _(pool):
            def body(mode, b):
                if mode == START:
                    masked.credit(pool, TL // 2)
                    mask_ready.credit(pool, 1)
                    stats_done.wait(pool, -1, 0)
                    pool.tensor_tensor(rstd[:, :], var_eps[:, :], half_pow[:, :], ALU.pow).then_inc(pow_done.sem, 1)
                if mode in WHOLE:
                    mask_in.wait(pool, b - 1, 0)
                    masked.wait(pool, b - 1, TL // 2 - 1)
                    pool.sem_inc(pool_waited, 1)
                    pool.tensor_scalar(maskb[:, :, :], mask_raw[:, :, :].bitcast(U8), MASKED, 1.0, ALU.mult, ALU.mult)\
                        .then_inc(mask_ready.sem, 1)
                    mask_ready.wait(pool, b, 0)
                    for u in range(TL // 2):
                        if u == 16 and mode != LAST:
                            stats_done.wait(pool, b, 0)
                            pool.tensor_tensor(rstd[:, :], var_eps[:, :], half_pow[:, :], ALU.pow).then_inc(pow_done.sem, 1)
                        j, half = u // 2, u % 2
                        s = u % 4
                        bias_in[s].wait(pool, b, u // 4)
                        tile = biasm[:, j % 2, 2 * half:2 * half + 2, :]
                        pool.tensor_tensor(tile, tile, maskb[:, 2 * half:2 * half + 2, :], ALU.add).then_inc(masked.sem, 1)

            batches(pool, body)

        @block.tensor
        def _(pe):
            def bank_user(mode, b, j, f):
                k = order.index((j, f))
                while True:
                    k -= 2
                    if k >= 0:
                        if runs(mode, *order[k]):
                            return b, order[k][1]
                    else:
                        if mode == START:
                            return None
                        return b - 1, order[k][1]

            def wait_bank(mode, b, j, f):
                user = bank_user(mode, b, j, f)
                if user is not None:
                    ub, (kind, n) = user
                    if kind == "x":
                        xf_done.wait(pe, ub, n)
                    elif kind == "v":
                        v_done.wait(pe, ub, n)
                    else:
                        lo_done.wait(pe, ub, qk_order.index((kind, n)))

            def product(ps, wh, wl, xh, xl, done):
                for c in range(NC):
                    for n, (a, m) in enumerate(((wh, xh), (wl, xh), (wh, xl))):
                        mm = pe.matmul(ps, a(c), m(c), start=(c == 0 and n == 0), stop=(c == NC - 1 and n == 2))
                mm.then_inc(done.sem, 1)

            def fill(mode, b, j, f):
                kind, n = f
                ps = ps_fill[:, order.index((j, f)) % 2, :]
                wait_bank(mode, b, j, f)
                if kind == "x":
                    if n == 0:
                        normed.wait(pe, b, NT - 1)
                    for t in range(NT):
                        mm = pe.transpose(ps[:, t * P:(t + 1) * P], xn[:, t, n * P:(n + 1) * P], ident[:, :])
                    mm.then_inc(xt_done.sem, 1)
                elif kind == "v":
                    cols = slice(n * P, (n + 1) * P)
                    product(ps, lambda c: XH[:, c, cols], lambda c: XL[:, c, cols],
                            lambda c: WH[2][:, c, :], lambda c: WL[2][:, c, :], vproj_done)
                else:
                    q = "qk".index(kind)
                    ahead, g, _ = group_of(f)
                    cols = slice(g * P, (g + 1) * P)
                    if f == ("q", NG):
                        xl_done.wait(pe, b, NC - 1)
                        xh_done.wait(pe, b, NC - 1)
                    product(ps, lambda c: WH[q][:, c, cols], lambda c: WL[q][:, c, cols],
                            lambda c: XH[:, c, :], lambda c: XL[:, c, :], proj_done)

            def body(mode, b):
                if mode == START:
                    scored.credit(pe, TL)
                    turned.credit(pe, TL)
                    pv_done.credit(pe, NG * NT + NT)
                    proj_done.credit(pe, 2 * NG - 3)
                    vproj_done.credit(pe, NT)
                    rt_done.credit(pe, NG + 1)
                for j, i in slots(mode):
                    g, h = j // GH, j % GH
                    before = group_before(mode, b, g)
                    if before is not None and h == 0:
                        pb, pg = before
                        ((outT_act if i % 2 == 0 else outT_dve)
                         .wait(pe, pb, 2 * (GH * pg + GH - 1) + i // 2))
                        if i == 0:
                            ctx_done.wait(pe, b - 1 if g == 0 else b, NG - 1 if g == 0 else g - 1)
                            v_done.wait(pe, pb, NT - 1)
                        for hh in range(GH):
                            head = GH * pg + hh
                            mm = pe.matmul(ps_ctx[HD * hh:HD * (hh + 1), 0, :], V[:, i, HD * head:HD * (head + 1)],
                                           probT[:, hh, i, :], start=(i == 0), stop=(i == NT - 1),
                                           skip_group_check=True)
                        mm.then_inc(pv_done.sem, 1)
                    t = score_tile(mode, b, j, i)
                    if t is not None:
                        sb_, sj, si = t
                        n = NT * sj + si
                        sg = sj // GH
                        if n >= 2:
                            maxed.wait(pe, sb_, n - 2)
                        else:
                            maxed.wait(pe, sb_ - 1, TL - 2 + n)
                        if sj % GH == 0 and si == 0:
                            for q in range(2):
                                rb, ri = rows_event(q, sb_, sg)
                                rows_in[q][sg % 2].wait(pe, rb, ri)
                        pe.matmul(ps_score[:, n % 2, :], stacked[0][sg % 2][:, sj % GH, si * P:(si + 1) * P],
                                  stacked[1][sg % 2][:, sj % GH, :], start=True, stop=True).then_inc(scored.sem, 1)
                    if mode in WHOLE:
                        n = NT * j + i
                        if i == 0:
                            exped.wait(pe, b, NT * j + NT - 1)
                        if n >= 2:
                            (outT_act if i % 2 == 0 else outT_dve).wait(pe, b, 2 * (j if i >= 2 else j - 1) + (0 if i >= 2 else 1))
                        else:
                            (outT_act if i % 2 == 0 else outT_dve).wait(pe, b - 1, TL // 2 - 1)
                        for tq in range(NT):
                            mm = pe.transpose(ps_probT[:, n % 2, tq * P:(tq + 1) * P],
                                              prob[:, j % 2, tq, i * P:(i + 1) * P], ident[:, :])
                        mm.then_inc(turned.sem, 1)
                    for f in fills_at(mode, j, i):
                        fill(mode, b, j, f)
                    if h == 0 and i == 3 and before is not None:
                        wide_done.wait(pe, b, g)
                        if g == 0:
                            rt_out.wait(pe, b - 1, NG - 1)
                        else:
                            rt_out.wait(pe, b, g - 1)
                        for tq in range(NT):
                            mm = pe.transpose(ps_rsum[:, 0, tq * P:(tq + 1) * P],
                                              rsum_wide[:, tq, :, :].rearrange("p h d -> p (h d)"), ident[:, :])
                        mm.then_inc(rt_done.sem, 1)

            batches(pe, body)

        @block.scalar
        def _(act):
            def body(mode, b):
                if mode == START:
                    exped.credit(act, TL)
                    outT_act.credit(act, TL // 2)
                    hi_done.credit(act, 2 * NG - 3)
                    rt_out.credit(act, NG + 1)
                for j, i in slots(mode):
                    g, h = j // GH, j % GH
                    if mode in WHOLE and i % 2 == 0:
                        turned.wait(act, b, NT * j + i)
                        if h == 0:
                            pv_done.wait(act, b, NT * g + i)
                        act.activation(probT[:, h, i, :], ps_probT[:, i % 2, :], ACT.Copy).then_inc(outT_act.sem, 1)
                    t = score_tile(mode, b, j, i)
                    if t is not None:
                        tb, tj, ti = t
                        maxed.wait(act, tb, NT * tj + ti)
                        e = act.activation(prob[:, tj % 2, ti, :], prob[:, tj % 2, ti, :], ACT.Exp,
                                           bias=negmax[:, tj % 2, ti:ti + 1], scale=-1.0,
                                           accum_out=sums[:, (tj // GH) % 2, ti, tj % GH:tj % GH + 1])
                        e.then_inc(exped.sem, 1)
                    for f in fills_at(mode, j, i):
                        kind, n = f
                        ps = ps_fill[:, order.index((j, f)) % 2, :]
                        if kind == "x":
                            xt_done.wait(act, b, n)
                            if n == 0:
                                mod_done.wait(act, b, 0)
                            if n >= 2:
                                xl_done.wait(act, b, n - 2)
                                xh_done.wait(act, b, n - 2)
                                xmod_out[n % 2].wait(act, b, 0)
                            elif mode != START:
                                xl_done.wait(act, b - 1, n + 2)
                                xh_done.wait(act, b - 1, n + 2)
                                xmod_out[n % 2].wait(act, b - 1, 1)
                            act.activation(xf[:, n % 2, :], ps, ACT.Identity, bias=mod_now[:, 1, n:n + 1],
                                           scale=mod_now[:, 0, n:n + 1]).then_inc(xf_done.sem, 1)
                            xf_done.wait(act, b, n)
                            if n == 0 and mode != START:
                                proj_done.wait(act, b, qk_order.index(("k", NG - 1)))
                                vproj_done.wait(act, b, NT - 1)
                            act.activation(XH[:, n, :], xf[:, n % 2, :], ACT.Copy).then_inc(xh_done.sem, 1)
                        elif kind in "qk":
                            q = "qk".index(kind)
                            m = qk_order.index(f)
                            _, gg, buf = group_of(f)
                            proj_done.wait(act, b, m)
                            prev = previous_rows(mode, b, f)
                            if prev is not None:
                                prev[0].wait(act, prev[1], prev[2])
                            act.activation(hi[q][:, :], ps, ACT.Identity, bias=bqk[:, q, gg:gg + 1])\
                                .then_inc(hi_done.sem, 1)
                    if h == 1 and i == 0 and group_before(mode, b, g) is not None:
                        rt_done.wait(act, b, g)
                        ctx_out[g % 2].wait(act, b - 1 if g < 2 else b, NG // 2 - 1 if g < 2 else 0)
                        act.activation(rsumT[:, g % 2, :], ps_rsum[:, 0, :], ACT.Copy).then_inc(rt_out.sem, 1)

            batches(act, body)

        @block.vector
        def _(dve):
            def norm_stats(b):
                x_in.wait(dve, b, 0)
                for t in range(NT):
                    dve.bn_stats(stats[:, t, :], xn[:, t, :]).then_inc(dve_step, 1)

            def norm_aggr(b):
                dve.wait_ge(dve_step, steps_at(b, NT))
                dve.sem_inc(dve_waited, 1)
                for t in range(NT):
                    dve.bn_aggr(mean_var[:, t, :], stats[:, t, :]).then_inc(dve_step, 1)
                dve.wait_ge(dve_step, steps_at(b, 2 * NT))
                dve.tensor_scalar(var_eps[:, :], mean_var[:, :, 1], EPS, None, ALU.add).then_inc(stats_done.sem, 1)

            def norm_apply(mode, b):
                pow_done.wait(dve, b, 0)
                for t in range(NT):
                    dve.tensor_scalar(xn[:, t, :], xn[:, t, :], mean_var[:, t, 0:1], rstd[:, t:t + 1],
                                      ALU.subtract, ALU.mult).then_inc(normed.sem, 1)
                if mode != START:
                    xf_done.wait(dve, b - 1, NC - 1)
                dve.tensor_copy(mod_now[:, :, :], mod[:, :, :, bass.ds(b + 1, 1)].rearrange("p a c o -> p a (c o)"))\
                    .then_inc(mod_done.sem, 1)

            def steps_at(b, n):
                return (b + 1) * (2 * NT) + n

            def body(mode, b):
                if mode == START:
                    maxed.credit(dve, TL)
                    outT_dve.credit(dve, TL // 2)
                    lo_done.credit(dve, 2 * NG - 3)
                    v_done.credit(dve, NT)
                    wide_done.credit(dve, NG + 1)
                    rsum_done.credit(dve, NG + 1)
                    ctx_done.credit(dve, NG + 1)
                for j, i in slots(mode):
                    g, h = j // GH, j % GH
                    if mode in AHEAD:
                        if (j, i) == (5, 0):
                            norm_stats(b)
                        if (j, i) == (6, 0):
                            norm_aggr(b)
                        if (j, i) == (8, 2):
                            norm_apply(mode, b)
                    t = score_tile(mode, b, j, i)
                    if t is not None:
                        tb, tj, ti = t
                        n = NT * tj + ti
                        scored.wait(dve, tb, n)
                        masked.wait(dve, tb, n // 2)
                        if ti == 0:
                            if tj >= 2:
                                turned.wait(dve, tb, NT * (tj - 2) + NT - 1)
                            else:
                                turned.wait(dve, tb - 1, NT * (tj + H - 2) + NT - 1)
                        dve.sem_inc(dve_waited, 1)
                        dve.tensor_tensor_reduce(prob[:, tj % 2, ti, :], ps_score[:, n % 2, :], biasm[:, tj % 2, ti, :],
                                                 -1.0, LOWEST, ALU.add, ALU.min,
                                                 negmax[:, tj % 2, ti:ti + 1]).then_inc(maxed.sem, 1)
                    if mode in WHOLE and i % 2 == 1:
                        turned.wait(dve, b, NT * j + i)
                        if h == 0:
                            pv_done.wait(dve, b, NT * g + i)
                        dve.tensor_copy(probT[:, h, i, :], ps_probT[:, i % 2, :]).then_inc(outT_dve.sem, 1)
                    for f in fills_at(mode, j, i):
                        kind, n = f
                        ps = ps_fill[:, order.index((j, f)) % 2, :]
                        if kind == "x":
                            xh_done.wait(dve, b, n)
                            dve.tensor_tensor(XL[:, n, :], xf[:, n % 2, :], XH[:, n, :].bitcast(F32), ALU.subtract)\
                                .then_inc(xl_done.sem, 1)
                        elif kind == "v":
                            vproj_done.wait(dve, b, n)
                            if n == 0:
                                pv_done.wait(dve, b, NT - 1)
                            dve.tensor_tensor(V[:, n, :], ps, bv_rows[:, :], ALU.add).then_inc(v_done.sem, 1)
                        else:
                            q = "qk".index(kind)
                            _, gg, _ = group_of(f)
                            hi_done.wait(dve, b, qk_order.index(f))
                            dve.scalar_tensor_tensor(lo[q][:, :], ps, bqk[:, q, gg:gg + 1], hi[q][:, :].bitcast(F32),
                                                     ALU.add, ALU.subtract).then_inc(lo_done.sem, 1)
                    before = group_before(mode, b, g)
                    if before is not None:
                        if h == 0 and i == 1:
                            pb, pg = before
                            exped.wait(dve, pb, NT * GH * (pg + 1) - 1)
                            dve.reciprocal(rsum[:, :, :], sums[:, pg % 2, :, :]).then_inc(rsum_done.sem, 1)
                            rsum_done.wait(dve, b, g)
                            rt_done.wait(dve, b - 1 if g == 0 else b, NG - 1 if g == 0 else g - 1)
                            dve.tensor_copy(rsum_wide[:, :, :, :],
                                            rsum[:, :, :].unsqueeze(3).broadcast_to([P, NT, GH, HD]))\
                                .then_inc(wide_done.sem, 1)
                        if h == 1 and i == 1:
                            pv_done.wait(dve, b, NT * g + NT - 1)
                            rt_out.wait(dve, b, g)
                            dve.tensor_tensor(rsumT[:, g % 2, :], ps_ctx[:, 0, :], rsumT[:, g % 2, :], ALU.mult)\
                                .then_inc(ctx_done.sem, 1)

            batches(dve, body)


def load_ffn_block(nc, W1, b1, W2, b2, g2, beta2, Wo, bo, W1H, W1L, W2H, W2L, wo, b1_all, b1_half, bo_col, b2_rows):
    D, F = W1.shape
    NC, NF = D // P, F // P
    with ExitStack() as local:
        def sb(name, shape, dt=F32):
            return local.enter_context(nc.sbuf_tensor(name, shape, dt))

        def sem(name):
            return local.enter_context(nc.semaphore(name))

        w1 = sb("w1_in", [P, NC, F])
        w2 = [sb(f"w2_in{i}", [P, NF // 4, D]) for i in range(2)]
        b1_in = sb("b1_in", [P, NF])
        g2_col, beta2_col = sb("g2_col", [P, NC]), sb("beta2_col", [P, NC])
        ps = local.enter_context(nc.psum_tensor("ps_load", [P, 512], F32))
        cols_in, rest_in = sem("cols_in"), sem("rest_in")
        w1_in = [sem(f"w1_in_sem{c}") for c in range(NC)]
        w2_in = [sem(f"w2_in_sem{c}") for c in range(2)]
        w1_hi, w2_hi, w2_lo, shifted, b1_sum = (sem(n) for n in ("w1_hi", "w2_hi", "w2_lo", "shifted", "b1_sum"))
        Q = NF // 4

        with nc.Block() as block:

            @block.sync
            def _(sp):
                for tile, src in ((g2_col, g2), (beta2_col, beta2), (b1_in, b1), (bo_col, bo)):
                    sp.dma_start(tile[:, :], src.rearrange("(c p) -> p c", p=P), allow_slow_non_contiguous=True)\
                        .then_inc(cols_in, 16)
                for c in range(NC):
                    sp.dma_start(w1[:, c, :], W1[c * P:(c + 1) * P, :]).then_inc(w1_in[c], 16)
                for q in range(4):
                    if q >= 2:
                        sp.wait_ge(w2_lo, Q * (q - 1))
                    sp.dma_start(w2[q % 2][:, :, :], W2[q * Q * P:(q + 1) * Q * P, :].rearrange("(c p) d -> p c d", p=P))\
                        .then_inc(w2_in[q % 2], 16)
                sp.dma_start(wo[:, :, :], Wo.rearrange("(c p) d -> p c d", p=P)).then_inc(rest_in, 16)
                sp.dma_start(b2_rows[:, :], b2.unsqueeze(0).broadcast_to([P, D])).then_inc(rest_in, 16)
                sp.wait_ge(rest_in, 32)

            @block.scalar
            def _(act):
                act.wait_ge(cols_in, 64)
                for c in range(NC):
                    act.wait_ge(w1_in[c], 16)
                    act.activation(W1H[:, c, :], w1[:, c, :], ACT.Copy, scale=g2_col[:, c:c + 1]).then_inc(w1_hi, 1)
                for f in range(NF):
                    q = f // Q
                    if f % Q == 0:
                        act.wait_ge(w2_in[q % 2], 16 * (q // 2 + 1))
                    act.activation(W2H[:, f, :], w2[q % 2][:, f % Q, :], ACT.Copy).then_inc(w2_hi, 1)

            @block.vector
            def _(dve):
                dve.wait_ge(cols_in, 64)
                for c in range(NC):
                    dve.wait_ge(w1_hi, c + 1)
                    dve.scalar_tensor_tensor(W1L[:, c, :], w1[:, c, :], g2_col[:, c:c + 1], W1H[:, c, :].bitcast(F32),
                                             ALU.mult, ALU.subtract)
                dve.wait_ge(shifted, 1)
                dve.tensor_tensor(b1_all[:, :], b1_in[:, :], ps[:, 0:NF], ALU.add).then_inc(b1_sum, 1)
                dve.wait_ge(b1_sum, 1)
                dve.tensor_scalar(b1_half[:, :], b1_all[:, :], SIGMOID_RATE / 2, None, ALU.mult)
                for f in range(NF):
                    q = f // Q
                    dve.wait_ge(w2_hi, f + 1)
                    dve.tensor_tensor(W2L[:, f, :], w2[q % 2][:, f % Q, :], W2H[:, f, :].bitcast(F32), ALU.subtract)\
                        .then_inc(w2_lo, 1)

            @block.tensor
            def _(pe):
                pe.wait_ge(cols_in, 64)
                for c in range(NC):
                    pe.wait_ge(w1_in[c], 16)
                for f in range(NF):
                    for c in range(NC):
                        mm = pe.matmul(ps[:, f:f + 1], w1[:, c, f * P:(f + 1) * P], beta2_col[:, c:c + 1],
                                       start=(c == 0), stop=(c == NC - 1))
                mm.then_inc(shifted, 1)


def ffn_stage(nc, stage, W1, b1, W2, b2, g2, beta2, Wo, bo, ident, rot, half_pow, ctx_dram, xmod_dram, out):
    B, S, D = out.shape
    F = W1.shape[1]
    NT, NC, NF = S // P, D // P, F // P
    assert B % 2 == 0

    def sb(name, shape, dt=F32):
        return stage.enter_context(nc.sbuf_tensor(name, shape, dt))

    def sem(name):
        return stage.enter_context(nc.semaphore(name))

    W1H, W1L = (sb(f"w1_{n}", [P, NC, F], F32R) for n in ("hi", "lo"))
    W2H, W2L = (sb(f"w2_{n}", [P, NF, D], F32R) for n in ("hi", "lo"))
    wo = sb("wo", [P, NC, D])
    b1_all, b1_half = sb("b1_all", [P, NF]), sb("b1_half", [P, NF])
    bo_col = sb("bo_col", [P, NC])
    b2_rows = sb("b2_rows", [P, D])
    load_ffn_block(nc, W1, b1, W2, b2, g2, beta2, Wo, bo, W1H, W1L, W2H, W2L, wo, b1_all, b1_half, bo_col, b2_rows)

    ctx = sb("ctx", [P, NC, S])
    yT = sb("y_t", [P, NC, S])
    HH, HL = (sb(f"h_{n}", [P, NC, S], F32R) for n in ("hi", "lo"))
    y2 = [sb(f"y_b2_{i}", [P, NT, D]) for i in range(2)]
    gate = sb("gate", [P, S])
    g = sb("g", [P, S])
    GHI, GLO = (sb(f"g_{n}", [P, 2, S], F32R) for n in ("hi", "lo"))
    turned_out = sb("turned_out", [P, 2, D // 4, 4])
    rot_now = sb("rot_now", [P, 6])
    stats = sb("stats2", [P, 6])
    mean_var = sb("mean_var2", [P, 2, 2])
    var_eps = sb("var_eps2", [P, 2])
    rstd = sb("rstd2", [P, 2])

    ps_y = stage.enter_context(nc.psum_tensor("ps_y", [P, 2, 512], F32))
    ps_h = stage.enter_context(nc.psum_tensor("ps_h", [P, 2, 512], F32))
    ps_out = stage.enter_context(nc.psum_tensor("ps_out", [P, NT, 512], F32))

    dve_waited, pool_waited = sem("dve_waited2"), sem("pool_waited2")
    ctx_in = Tally(sem("ctx_in"), 1, 16)
    xmod_in = Tally(sem("xmod_in"), 1, 16)
    projected = Tally(sem("projected"), NC)
    yT_done = Tally(sem("yT_done"), NC)
    y_done = Tally(sem("y_done"), NT)
    ln_step = Tally(sem("ln_step"), 2 * NT)
    var_done = Tally(sem("var_done"), NT)
    pow_done = Tally(sem("pow_done2"), NT)
    z_done = Tally(sem("z_done"), NT)
    zT_done = Tally(sem("zT_done"), NC)
    hh_done = Tally(sem("hh_done"), NC)
    hl_done = Tally(sem("hl_done"), NC)
    ffn1 = Tally(sem("ffn1"), NF)
    tanh_done = Tally(sem("tanh_done"), NF)
    gate_done = Tally(sem("gate_done"), NF)
    g_done = Tally(sem("g_done"), NF)
    ghi_done = Tally(sem("ghi_done"), NF)
    glo_done = Tally(sem("glo_done"), NF)
    ffn2 = Tally(sem("ffn2"), NF * NT)
    sum_done = Tally(sem("sum_done"), NT)
    rot_picked = Tally(sem("rot_picked"), 1)
    crossed = Tally(sem("crossed"), NT)
    rotated = Tally(sem("rotated"), NT)
    out_done = [Tally(sem(f"out_done{i}"), NT // 2, 16) for i in range(2)]

    START, FIRST, MIDDLE, LAST, END = "start", "first", "middle", "last", "end"
    WHOLE = (FIRST, MIDDLE, LAST)
    AHEAD = (START, FIRST, MIDDLE)
    LAG = 2
    project_at = {2: 0, 4: 1, 6: 2, 8: 3}
    y_at = {9: 0, 10: 1, 11: 2, 12: 3}
    z_at = {10: 0, 11: 1, 12: 2, 13: 3}
    h_at = {NF - 1: (0, 1), NF: (2,), NF + 1: (3,)}

    def batches(eng, body):
        body(START, -1, 1)
        body(FIRST, 0, 0)
        with eng.Fori(0, (B - 2) // 2) as i:
            body(MIDDLE, i * 2 + 1, 1)
            body(MIDDLE, i * 2 + 2, 0)
        body(LAST, B - 1, 1)
        body(END, B, 0)

    with nc.Block() as block:

        @block.sync
        def _(sp):
            def body(mode, b, par):
                if mode == START:
                    for s in range(2):
                        out_done[s].credit(sp, NT)
                if mode in AHEAD:
                    if mode != START:
                        zT_done.wait(sp, b - 1, NC - 1)
                    sp.dma_start(ctx[:, :, :], ctx_dram[bass.ds(b + 1, 1), :, :].rearrange("o (c p) s -> p (o c) s", p=P))\
                        .then_inc(ctx_in.sem, 16)
                    sp.dma_start(yT[:, :, :], xmod_dram[bass.ds(b + 1, 1), :, :].rearrange("o (c p) s -> p (o c) s", p=P))\
                        .then_inc(xmod_in.sem, 16)
                if mode in (MIDDLE, LAST, END):
                    for t in range(NT):
                        rotated.wait(sp, b, t)
                        sp.dma_start(out[bass.ds(b - 1, 1), t * P:(t + 1) * P, :].rearrange("o p d -> p (o d)"),
                                     turned_out[:, t % 2, :, :].rearrange("p q r -> p (q r)"))\
                            .then_inc(out_done[t % 2].sem, 16)
                if mode == END:
                    for s in range(2):
                        out_done[s].wait(sp, B, NT // 2 - 1)

            batches(sp, body)

        @block.tensor
        def _(pe):
            def wait_ps_y(mode, b, k):
                k -= 2
                if k < 0:
                    if mode != START:
                        hl_done.wait(pe, b - 1, NC + k)
                elif k < 4:
                    yT_done.wait(pe, b, k)
                elif k < 8:
                    z_done.wait(pe, b, k - 4)
                else:
                    hl_done.wait(pe, b, k - 8)

            def body(mode, b, par):
                if mode == START:
                    ffn1.credit(pe, NF)
                    ffn2.credit(pe, NF * NT)
                for f in range(NF + LAG):
                    if mode in AHEAD and f in project_at:
                        o = project_at[f]
                        wait_ps_y(mode, b, o)
                        if o == 0:
                            ctx_in.wait(pe, b, 0)
                        for c in range(NC):
                            mm = pe.matmul(ps_y[:, o % 2, :], wo[:, c, o * P:(o + 1) * P], ctx[:, c, :],
                                           start=(c == 0), stop=(c == NC - 1))
                        mm.then_inc(projected.sem, 1)
                    if mode in AHEAD and f in y_at:
                        t = y_at[f]
                        wait_ps_y(mode, b, 4 + t)
                        if t == 0:
                            yT_done.wait(pe, b, NC - 1)
                        for c in range(NC):
                            mm = pe.transpose(ps_y[:, t % 2, c * P:(c + 1) * P], yT[:, c, t * P:(t + 1) * P], ident[:, :])
                        mm.then_inc(y_done.sem, 1)
                    if mode in WHOLE and f < NF:
                        if f == 0:
                            hl_done.wait(pe, b - 1, NC - 1)
                            hh_done.wait(pe, b - 1, NC - 1)
                        g_done.wait(pe, b if f >= 2 else b - 1, f - 2 if f >= 2 else NF - 2 + f)
                        for c in range(NC):
                            for n, (w, h) in enumerate(((W1H, HH), (W1L, HH), (W1H, HL))):
                                mm = pe.matmul(ps_h[:, f % 2, :], w[:, c, f * P:(f + 1) * P], h[:, c, :],
                                               start=(c == 0 and n == 0), stop=(c == NC - 1 and n == 2))
                        mm.then_inc(ffn1.sem, 1)
                    if mode in AHEAD and f in h_at:
                        for c in h_at[f]:
                            wait_ps_y(mode, b, 8 + c)
                            if c == 0:
                                z_done.wait(pe, b, NT - 1)
                            for t in range(NT):
                                mm = pe.transpose(ps_y[:, c % 2, t * P:(t + 1) * P], ctx[:, t, c * P:(c + 1) * P],
                                                  ident[:, :])
                            mm.then_inc(zT_done.sem, 1)
                    if mode in WHOLE and f >= LAG:
                        n = f - LAG
                        ghi_done.wait(pe, b, n)
                        glo_done.wait(pe, b, n)
                        for t in range(NT):
                            if n == 0:
                                sum_done.wait(pe, b - 1, t)
                            cols = slice(t * P, (t + 1) * P)
                            for k, (a, w) in enumerate(((GHI, W2H), (GLO, W2H), (GHI, W2L))):
                                mm = pe.matmul(ps_out[:, t, :], a[:, n % 2, cols], w[:, n, :],
                                               start=(n == 0 and k == 0), stop=(n == NF - 1 and k == 2))
                            mm.then_inc(ffn2.sem, 1)

            batches(pe, body)

        @block.scalar
        def _(act):
            def body(mode, b, par):
                if mode == START:
                    tanh_done.credit(act, NF)
                    ghi_done.credit(act, NF)
                for f in range(NF + LAG):
                    if mode in WHOLE and f < NF:
                        ffn1.wait(act, b, f)
                        ghi_done.wait(act, b if f else b - 1, f - 1 if f else NF - 1)
                        g_done.wait(act, b if f else b - 1, f - 1 if f else NF - 1)
                        act.activation(gate[:, :], ps_h[:, f % 2, :], ACT.Tanh, bias=b1_half[:, f:f + 1],
                                       scale=SIGMOID_RATE / 2).then_inc(tanh_done.sem, 1)
                        ffn2.wait(act, b if f >= 2 else b - 1, NT * ((f - 2) if f >= 2 else NF - 2 + f) + NT - 1)
                        g_done.wait(act, b, f)
                        act.activation(GHI[:, f % 2, :], g[:, :], ACT.Copy).then_inc(ghi_done.sem, 1)
                    if mode in AHEAD and f in h_at:
                        for c in h_at[f]:
                            zT_done.wait(act, b, c)
                            act.activation(HH[:, c, :], ps_y[:, c % 2, :], ACT.Copy).then_inc(hh_done.sem, 1)

            batches(act, body)

        @block.gpsimd
        def _(pool):
            def body(mode, b, par):
                if mode == START:
                    glo_done.credit(pool, NF)
                    crossed.credit(pool, 2 * NT)
                for f in range(NF + LAG):
                    if mode in (MIDDLE, LAST, END) and f < NT:
                        sum_done.wait(pool, b - 1, f)
                        if f == 0:
                            rot_picked.wait(pool, b, 0)
                        out_done[f % 2].wait(pool, b if f >= 2 else b - 1, 0 if f >= 2 else NT // 2 - 1)
                        y = y2[1 - par][:, f, :].rearrange("p (q r) -> p q r", r=4)
                        o = turned_out[:, f % 2, :, :]
                        pool.sem_inc(pool_waited, 1)
                        for n in range(2):
                            pool.tensor_scalar(o[:, :, 2 * n], y[:, :, 2 * n + 1], rot_now[:, n:n + 1], None, ALU.mult)
                            mm = pool.tensor_scalar(o[:, :, 2 * n + 1], y[:, :, 2 * n], rot_now[:, 4 + n:5 + n], None, ALU.mult)
                        mm.then_inc(crossed.sem, 1)
                    if mode in WHOLE and f < NF:
                        ghi_done.wait(pool, b, f)
                        pool.tensor_tensor(GLO[:, f % 2, :], g[:, :], GHI[:, f % 2, :].bitcast(F32), ALU.subtract)\
                            .then_inc(glo_done.sem, 1)
                    if mode in AHEAD and f in y_at:
                        t = y_at[f]
                        var_done.wait(pool, b, t)
                        pool.tensor_tensor(rstd[:, t % 2:t % 2 + 1], var_eps[:, t % 2:t % 2 + 1], half_pow[:, 0:1],
                                           ALU.pow).then_inc(pow_done.sem, 1)

            batches(pool, body)

        @block.vector
        def _(dve):
            def body(mode, b, par):
                if mode == START:
                    gate_done.credit(dve, NF)
                    g_done.credit(dve, NF)
                    sum_done.credit(dve, NT)
                    rot_picked.credit(dve, 2)
                    rotated.credit(dve, 2 * NT)
                if mode in (MIDDLE, LAST, END):
                    rotated.wait(dve, b - 1, NT - 1)
                    dve.tensor_copy(rot_now[:, :], rot[:, :, bass.ds(b - 1, 1)].rearrange("p a o -> p (a o)"))\
                        .then_inc(rot_picked.sem, 1)
                for f in range(NF + LAG):
                    if mode in WHOLE and f < NF:
                        tanh_done.wait(dve, b, f)
                        dve.scalar_tensor_tensor(gate[:, :], ps_h[:, f % 2, :], b1_all[:, f:f + 1], gate[:, :],
                                                 ALU.add, ALU.mult).then_inc(gate_done.sem, 1)
                        gate_done.wait(dve, b, f)
                        glo_done.wait(dve, b if f else b - 1, f - 1 if f else NF - 1)
                        dve.scalar_tensor_tensor(g[:, :], ps_h[:, f % 2, :], b1_all[:, f:f + 1], gate[:, :],
                                                 ALU.add, ALU.add).then_inc(g_done.sem, 1)
                    if mode in (MIDDLE, LAST, END) and f < NT:
                        crossed.wait(dve, b, f)
                        y = y2[1 - par][:, f, :].rearrange("p (q r) -> p q r", r=4)
                        o = turned_out[:, f % 2, :, :]
                        for n in range(2):
                            mm = dve.scalar_tensor_tensor(o[:, :, 2 * n:2 * n + 2], y[:, :, 2 * n:2 * n + 2],
                                                          rot_now[:, 2 + n:3 + n], o[:, :, 2 * n:2 * n + 2],
                                                          ALU.mult, ALU.add)
                        mm.then_inc(rotated.sem, 1)
                    if mode in AHEAD and f in project_at:
                        o = project_at[f]
                        projected.wait(dve, b, o)
                        if o == 0:
                            xmod_in.wait(dve, b, 0)
                        dve.scalar_tensor_tensor(yT[:, o, :], ps_y[:, o % 2, :], bo_col[:, o:o + 1], yT[:, o, :],
                                                 ALU.add, ALU.add).then_inc(yT_done.sem, 1)
                    if mode in AHEAD and f in z_at:
                        t = z_at[f]
                        pow_done.wait(dve, b, t)
                        dve.tensor_scalar(ctx[:, t, :], ps_y[:, t % 2, :], mean_var[:, t % 2, 0:1],
                                          rstd[:, t % 2:t % 2 + 1], ALU.subtract, ALU.mult).then_inc(z_done.sem, 1)
                    if mode in AHEAD and f in y_at:
                        t = y_at[f]
                        y_done.wait(dve, b, t)
                        dve.bn_stats(stats[:, :], ps_y[:, t % 2, :]).then_inc(ln_step.sem, 1)
                        dve.tensor_tensor(y2[1 - par][:, t, :], ps_y[:, t % 2, :], b2_rows[:, :], ALU.add)
                        ln_step.wait(dve, b, 2 * t)
                        dve.sem_inc(dve_waited, 1)
                        dve.bn_aggr(mean_var[:, t % 2, :], stats[:, :]).then_inc(ln_step.sem, 1)
                        ln_step.wait(dve, b, 2 * t + 1)
                        dve.tensor_scalar(var_eps[:, t % 2:t % 2 + 1], mean_var[:, t % 2, 1:2], EPS, None, ALU.add)\
                            .then_inc(var_done.sem, 1)
                    if mode in AHEAD and f in h_at:
                        for c in h_at[f]:
                            hh_done.wait(dve, b, c)
                            dve.tensor_tensor(HL[:, c, :], ps_y[:, c % 2, :], HH[:, c, :].bitcast(F32), ALU.subtract)\
                                .then_inc(hl_done.sem, 1)
                    if mode in WHOLE and f == NF + LAG - 1:
                        for t in range(NT):
                            ffn2.wait(dve, b, NT * (NF - 1) + t)
                            dve.scalar_tensor_tensor(y2[par][:, t, :], ps_out[:, t, :], 0.5, y2[par][:, t, :],
                                                     ALU.mult, ALU.add).then_inc(sum_done.sem, 1)

            batches(dve, body)


_INS = ['x', 'itok_B_34_63', 'fside_Bx16xSxS_0', 'condB_theta', 'condB_phi', 'mask_Bx1xSxS_bk0', 'L0_cond_W_ada',
        'L0_cond_b_ada', 'L0_cond_Wq', 'L0_cond_bq', 'L0_cond_Wk', 'L0_cond_bk', 'L0_cond_Wv', 'L0_cond_bv',
        'L0_cond_Wo', 'L0_cond_bo', 'L0_cond_W1', 'L0_cond_b1', 'L0_cond_W2', 'L0_cond_b2', 'L0_cond_g2',
        'L0_cond_beta2']


def arrays_of(inputs):
    arrays = {}
    for name in _INS:
        a = np.ascontiguousarray(inputs[name])
        arrays[name] = a.view(np.int32) if a.dtype == np.bool_ else a
    half = arrays['x'].shape[2] // 2
    exponents = np.arange(half, dtype=np.float32) * np.float32(-math.log(10000.0) / (half - 1))
    arrays['freqs'] = np.exp(exponents.astype(np.float64)).astype(np.float32)
    return arrays


def kernel(**inputs):
    import concourse.bacc as _bacc
    from concourse.bass_utils import run_bass_kernel_spmd as _run

    nc = _bacc.Bacc("TRN2", target_bir_lowering=False, num_devices=1)
    arrays, args = {}, []
    for name, a in arrays_of(inputs).items():
        arrays[f"in_{name}_dram"] = a
        args.append(nc.dram_tensor(f"in_{name}_dram", a.shape, mybir.dt.from_np(a.dtype), kind="ExternalInput").ap())
    out = nc.dram_tensor("out_0_dram", inputs['x'].shape, F32, kind="ExternalOutput").ap()
    layer_program(nc, *args, out)
    return _run(nc, [arrays], core_ids=[0]).results[0]["out_0_dram"]
```
